# Optimizing a Trainium2 kernel written in Bass

```python
import numpy as np
import jax
import jax.numpy as jnp

def _softmax(x, axis=-1):
    return jax.nn.softmax(x, axis=axis)

def _gelu(x):
    return jax.nn.gelu(x, approximate=True)

def _silu(x):
    return jax.nn.silu(x)

def _sigmoid(x):
    return jax.nn.sigmoid(x)

def _layernorm(x, axis=-1, eps=1e-05):
    m = jnp.mean(x, axis=axis, keepdims=True)
    v = jnp.var(x, axis=axis, keepdims=True)
    return (x - m) / jnp.sqrt(v + eps)

def _scatter_add(tgt, idx, src, axis=0):
    return tgt.at[idx].add(src)

def _segment_sum(src, seg, n):
    return jax.ops.segment_sum(src, seg, n)
kernel_name = 'mk_cond_seq_d1_seqx_r2_18eb6f'

def setup_inputs(seed: int=0):
    np.random.seed(seed)
    _w = jnp.asarray

    def _rec_inputs():
        import jax
        import jax.numpy as jnp
        _rk = jax.random.key(seed)
        x = -0.0003929 + 0.9999 * jax.random.normal(jax.random.fold_in(_rk, 1), (8, 512, 512), jnp.float32)
        _lenS = 512 - jax.random.randint(jax.random.fold_in(_rk, 7), (8,), 0, max(1, 512 // 4) + 1, jnp.int32)
        _lenS2 = 512 - jax.random.randint(jax.random.fold_in(_rk, 8), (8,), 0, max(1, 512 // 4) + 1, jnp.int32)
        cond_256 = -0.0209273 + 1.04763 * jax.random.normal(jax.random.fold_in(_rk, 11), (8, 128), jnp.float32)
        return (x, cond_256)
    x, cond_256 = _rec_inputs()

    def _L0_cond_setup():
        import jax, jax.numpy as jnp
        import numpy as np
        EPS = 1e-06

        def act_quant(x):
            scale = 127.0 / jnp.clip(jnp.max(jnp.abs(x), axis=-1, keepdims=True), 1e-05, None)
            return jnp.clip(jnp.round(x * scale), -128.0, 127.0) / scale

        def weight_quant(w):
            scale = 1.0 / jnp.clip(jnp.mean(jnp.abs(w)), 1e-05, None)
            return jnp.clip(jnp.round(w * scale), -1.0, 1.0) / scale
        key = jax.random.key(seed)
        k0, k1, k2, k3, k4 = jax.random.split(key, 5)
        B, S, D, FF, C = (4, 2048, 512, 2048, 128)
        return {'x': jax.random.normal(k0, (B, S, D), jnp.float32), 'cond': jax.random.normal(k1, (B, C), jnp.float32), 'norm_w': jax.random.normal(k2, (D, C), jnp.float32) * 0.02, 'up_w': jax.random.normal(k3, (2 * FF, D), jnp.float32) * 0.02, 'down_w': jax.random.normal(k4, (D, FF), jnp.float32) * 0.02}
    _L0_cond_all = _L0_cond_setup()
    _L0_cond_in = {k: v for k, v in _L0_cond_all.items() if k in ('norm_w', 'up_w', 'down_w')}
    del _L0_cond_all
    return {'x': x, 'cond_256': cond_256, 'L0_cond_norm_w': _L0_cond_in['norm_w'], 'L0_cond_up_w': _L0_cond_in['up_w'], 'L0_cond_down_w': _L0_cond_in['down_w']}

def reference(x, cond_256, L0_cond_norm_w, L0_cond_up_w, L0_cond_down_w):
    import jax
    import jax.numpy as jnp

    def _L0_cond_ref(x, cond, norm_w, up_w, down_w):
        import jax, jax.numpy as jnp
        import numpy as np
        EPS = 1e-06

        def act_quant(x):
            scale = 127.0 / jnp.clip(jnp.max(jnp.abs(x), axis=-1, keepdims=True), 1e-05, None)
            return jnp.clip(jnp.round(x * scale), -128.0, 127.0) / scale

        def weight_quant(w):
            scale = 1.0 / jnp.clip(jnp.mean(jnp.abs(w)), 1e-05, None)
            return jnp.clip(jnp.round(w * scale), -1.0, 1.0) / scale
        scale = cond @ norm_w.T + 1.0
        ms = jnp.mean(x * x, axis=-1, keepdims=True)
        h = x * (scale[:, None, :] * jax.lax.rsqrt(ms + EPS))
        u = h @ up_w.T
        val, gate = jnp.split(u, 2, axis=-1)
        h = val * jax.nn.gelu(gate, approximate=False)
        hq = h + jax.lax.stop_gradient(act_quant(h) - h)
        wq = down_w + jax.lax.stop_gradient(weight_quant(down_w) - down_w)
        y = hq @ wq.T
        return y + x
    x = _L0_cond_ref(x, cond_256, L0_cond_norm_w, L0_cond_up_w, L0_cond_down_w)
    return x

_drawn_inputs = setup_inputs


def setup_inputs(seed=0):
    import zlib

    import numpy as np

    out = dict(_drawn_inputs(seed))
    spreads = {}
    factors = {}
    for name, (base, spread) in spreads.items():
        noise = np.random.default_rng([zlib.crc32(name.encode()), seed]).standard_normal(out[name].shape)
        drawn = base * np.exp(spread * noise) if base else spread * noise
        out[name] = jnp.asarray(drawn.astype(out[name].dtype))
    for name, factor in factors.items():
        out[name] = (out[name] * factor).astype(out[name].dtype)
    return out
```

```python
import concourse.bass as bass
from concourse import mybir
from contextlib import ExitStack


def gated_ffn_program(nc, x, cond, norm_w, up_w, down_w, out):
    F32, F16, I32 = mybir.dt.float32, mybir.dt.float16, mybir.dt.int32
    ALU, ACT, AX = mybir.AluOpType, mybir.ActivationFunctionType, mybir.AxisListType

    P = nc.NUM_PARTITIONS
    B, T, D = x.shape
    C = cond.shape[1]
    FF = down_w.shape[1]
    KT = D // P
    TT = T // P
    FT = FF // P
    VG = 2
    LAST = B - 1

    MAGIC = 1.5 * 2.0 ** 23
    EXPONENT = 0x7F800000
    TINY = 2.0 ** -100
    W_GAIN = 2.0 ** 13
    H_GAIN = 2.0 ** 9
    RMS_EPS = 1e-6
    QMAX, QMIN, QEPS = 127.0, -128.0, 1e-5

    EARLY = 4
    PAIRS = FT // 2
    QUANT_FROM = 1
    PAIR_ORDER = [(EARLY // 2 + i) % PAIRS for i in range(PAIRS)]
    XPREP_AT = {4 + k: k for k in range(KT)}
    DOWN_AFTER = {8: 0, 10: 1, 12: 2, 14: 3}
    MAX_GROUPS = [(0, 4), (4, 4), (8, 4), (12, 3), (15, 1)]
    MAX_OPS = 2 * len(MAX_GROUPS) - 1
    MAX_AFTER = {s + n - 1: j for j, (s, n) in enumerate(MAX_GROUPS)}
    WSTAGE = 3
    DW_LOAD = {3: 0, 4: 1, 5: 2, 6: 3}
    DW_SUM = {6: 0, 7: 1, 8: 2, 9: 3}
    DW_TOTAL = 10
    DW_TERN = {11: 0, 12: 1, 13: 2, 14: 3}
    DW_T = {12: 0, 13: 1, 14: 2, 15: 3}

    x_v = x.rearrange("b (t p) d -> b p t d", p=P)
    out_v = out.rearrange("b (t p) d -> b p t d", p=P)
    up_v = up_w.rearrange("(v s p) d -> s p v d", v=VG, p=P)
    dw_v = down_w.rearrange("(k p) f -> k p f", p=P)

    ctx = ExitStack()
    with ctx:
        def sb(name, shape, dt):
            return ctx.enter_context(nc.sbuf_tensor(name, shape, dt))

        def pb(name):
            return ctx.enter_context(nc.psum_tensor(name, [P, 512], F32))

        def sem(name):
            return ctx.enter_context(nc.semaphore(name))

        wT = sb("wT", [P, FT, VG, 2 * KT * P], F16)
        dT = sb("dT", [P, FT, D], F16)
        h = sb("h", [P, (FT + EARLY) * T], F32)
        q = sb("q", [P, FT * T], F16)
        xT = sb("xT", [P, 2 * 2 * KT * T], F16)
        xin = sb("xin", [P, TT, D], F32)
        xres = sb("xres", [P, 2, D], F32)
        g = sb("g", [P, 2, T], F32)
        m = sb("m", [P, T], F32)
        mpart = sb("mpart", [P, T], F32)
        junk = sb("junk", [P, FF], F16)
        ident = sb("ident", [P, P], F32)
        ident16 = sb("ident16", [P, P], F16)
        ones = sb("ones", [P, P], F32)
        c_w = sb("c_w", [P, FT * VG], F32)
        inv_w = sb("inv_w", [P, FT * VG], F32)
        c_all = sb("c_all", [P, B * FT * VG], F32)
        c_b = sb("c_b", [P, B], F32)
        inv_b = sb("inv_b", [P, B], F32)
        scl = sb("scl", [P, KT * B], F32)
        bmax = sb("bmax", [P, B], F32)
        brow = sb("brow", [B, 1], F32)
        ss, ms, neg_half, r_pow, r_a, r_b, rstd, amax, amax_inv, qscale, dq = [
            sb(n, [P, TT], F32) for n in
            "ss ms neg_half r_pow r_a r_b rstd amax amax_inv qscale dq".split()]
        dwsum = sb("dwsum", [P, KT], F32)
        dwmean, sw, mdq = [sb(n, [P, 1], F32) for n in ("dwmean", "sw", "mdq")]

        wst = sb("wst", [P, WSTAGE, VG, D], F32)
        whl = sb("whl", [P, 2, VG, 2 * D], F16)
        ystage = whl[:, 0, :, :].rearrange("p v n -> p (v n)").bitcast(F32).rearrange("p (a d) -> p a d", a=2)
        dw2 = sb("dw2", [P, FF], F32)
        q32 = q[:, :].bitcast(F32)
        dw = [q32[:, 0:FF], q32[:, FF:2 * FF], dw2[:, :], h[:, FT * T:(FT + EARLY) * T]]
        tern = xres[:, :, :].rearrange("p a d -> p (a d)").bitcast(F16)
        nw = h[:, (FT - 1) * T:FT * T].rearrange("p (k c) -> p k c", k=KT)
        nwT = h[:, (FT - 2) * T:(FT - 1) * T].rearrange("p (k c) -> p k c", k=KT)
        cnd = h[0:B, (FT - 3) * T:(FT - 3) * T + C]
        cndT = h[:, (FT - 4) * T:(FT - 4) * T + B]

        def h_tiles(b, s, n):
            at = s * T + (b % 2 * FT * T if s < EARLY else 0)
            return h[:, bass.ds(at, n * T)]

        def xT_tile(b, part, k):
            return xT[:, bass.ds(b % 2 * (2 * KT * T) + (part * KT + k) * T, T)]

        def c_of(b, s, v):
            return c_all[:, bass.ds(b * (FT * VG) + (s * VG + v), 1)]

        def scl_of(b, k):
            return scl[:, bass.ds(b + k * B, 1)]

        def x_block(ap, b):
            return ap[b] if isinstance(b, int) else ap[bass.ds(b, 1)].rearrange("o p t d -> p (o t) d")

        def x_tile(ap, b, t):
            return ap[b, :, t, :] if isinstance(b, int) else ap[bass.ds(b, 1), :, t, :].rearrange("o p d -> p (o d)")

        V = [pb("V0"), pb("V1")]
        G = [pb("G0"), pb("G1")]
        X = pb("X")
        S = pb("S")
        Y = [pb("Y0"), pb("Y1")]
        WB = [S, Y[0], Y[1]]
        TAIL = [V[0], V[1], G[0], G[1]]

        consts_ready = sem("consts_ready")
        ident_steps = sem("ident_steps")
        cond_loaded = sem("cond_loaded")
        condT_psum = sem("condT_psum")
        condT_ready = sem("condT_ready")
        scl_psum = sem("scl_psum")
        scl_steps = sem("scl_steps")
        bmaxT_psum = sem("bmaxT_psum")
        bmax_psum = sem("bmax_psum")
        scl_ready = sem("scl_ready")
        x_loaded = sem("x_loaded")
        squares_ready = sem("squares_ready")
        ms_ready = sem("ms_ready")
        pow_ready = sem("pow_ready")
        newton_steps = sem("newton_steps")
        rstd_ready = sem("rstd_ready")
        xn_ready = sem("xn_ready")
        xT_psum = sem("xT_psum")
        xhi_ready = sem("xhi_ready")
        xlo_ready = sem("xlo_ready")
        w_loaded = [sem(f"w_loaded{i}") for i in range(WSTAGE)]
        w_steps = sem("w_steps")
        w_scale_ready = sem("w_scale_ready")
        whi_ready = sem("whi_ready")
        wlo_ready = sem("wlo_ready")
        wT_psum = sem("wT_psum")
        wT_ready = sem("wT_ready")
        c_ready = sem("c_ready")
        dw_loaded = [sem(f"dw_loaded{i}") for i in range(KT)]
        dw_sums = sem("dw_sums")
        dw_total_psum = sem("dw_total_psum")
        dw_steps = sem("dw_steps")
        dw_scale_ready = sem("dw_scale_ready")
        dw_scaled = sem("dw_scaled")
        dw_clipped = sem("dw_clipped")
        dw_rounded = sem("dw_rounded")
        dT_psum = sem("dT_psum")
        dT_ready = sem("dT_ready")
        gate_ready = sem("gate_ready")
        val_ready = sem("val_ready")
        gelu_done = sem("gelu_done")
        h_ready = sem("h_ready")
        max_ready = sem("max_ready")
        amaxT_psum = sem("amaxT_psum")
        amax_steps = sem("amax_steps")
        qscale_ready = sem("qscale_ready")
        dq_ready = sem("dq_ready")
        qscale_psum = sem("qscale_psum")
        q_scaled = sem("q_scaled")
        q_clipped = sem("q_clipped")
        q_ready = sem("q_ready")
        y_psum = sem("y_psum")
        y_done = sem("y_done")
        xres_loaded = [sem(f"xres_loaded{i}") for i in range(2)]
        ystage_free = [sem(f"ystage_free{i}") for i in range(2)]

        block = ctx.enter_context(nc.Block())

        @block.sync
        def _(sp):
            def load_w(p):
                if p >= WSTAGE:
                    sp.wait_ge(wlo_ready, VG * (p - WSTAGE + 1))
                sp.dma_start(wst[:, p % WSTAGE], up_v[p]).then_inc(w_loaded[p % WSTAGE], 16)

            def load_x(b):
                sp.dma_start(xin[:, :, :], x_block(x_v, b)).then_inc(x_loaded, 16)

            def load_xres(b, t):
                sp.dma_start(xres[:, t % 2, :], x_tile(x_v, b, t)).then_inc(xres_loaded[t % 2], 16)

            def store_y(b, t):
                sp.wait_ge(y_done, 4 * b + (t + 1))
                sp.dma_start(x_tile(out_v, b, t), ystage[:, t % 2, :]).then_inc(ystage_free[t % 2], 16)

            def results(b):
                load_xres(b, 0)
                load_xres(b, 1)
                for t in range(TT):
                    store_y(b, t)
                    if t + 2 < TT:
                        load_xres(b, t + 2)

            load_w(0)
            load_x(0)
            for p in range(1, WSTAGE):
                load_w(p)
            sp.wait_ge(xT_psum, KT)
            load_x(1)
            for s in range(FT):
                if s + WSTAGE < FT:
                    load_w(s + WSTAGE)
                if s in DW_LOAD:
                    k = DW_LOAD[s]
                    sp.dma_start(dw[k], dw_v[k]).then_inc(dw_loaded[k], 16)
            sp.wait_ge(dT_psum, 2 * KT)
            with sp.Fori(1, LAST) as b:
                sp.wait_ge(xT_psum, KT * b + KT)
                load_x(b + 1)
                results(b - 1)
            results(LAST - 1)
            results(LAST)
            for i in range(2):
                sp.wait_ge(ystage_free[i], 16 + 16 * B * TT // 2)

        @block.gpsimd
        def _(pool):
            pool.memset(ident[:, :], 0.0).then_inc(ident_steps, 1)
            pool.memset(ones[:, :], 1.0)
            pool.memset(neg_half[:, :], -0.5)
            pool.wait_ge(ident_steps, 1)
            pool.affine_select(out=ident[:, :], in_=ident[:, :], compare_op=ALU.not_equal, fill=1.0,
                               base=0, pattern=[[-1, P]], channel_multiplier=1).then_inc(ident_steps, 1)
            pool.wait_ge(ident_steps, 2)
            pool.tensor_copy(ident16[:, :], ident[:, :]).then_inc(consts_ready, 1)

            def rsqrt(b):
                pool.wait_ge(ms_ready, b + 1)
                pool.tensor_tensor(r_pow[:, :], ms[:, :], neg_half[:, :], ALU.pow).then_inc(pow_ready, 1)

            rsqrt(0)
            rsqrt(1)
            pool.wait_ge(dw_scale_ready, 1)
            for k in range(KT):
                pool.tensor_scalar(dw[k], dw[k], sw[:, 0:1], 1.0, ALU.mult, ALU.mult).then_inc(dw_scaled, 1)
                pool.wait_ge(dw_scaled, k + 1)
                pool.tensor_scalar(dw[k], dw[k], 1.0, -1.0, ALU.min, ALU.max).then_inc(dw_clipped, 1)
            with pool.Fori(1, LAST) as b:
                rsqrt(b + 1)

        @block.scalar
        def _(act):
            act.dma_start(nw, norm_w.rearrange("(k p) c -> p k c", p=P)).then_inc(cond_loaded, 16)
            act.dma_start(cnd, cond).then_inc(cond_loaded, 16)

            def squares(b):
                act.wait_ge(x_loaded, 16 * b + 16)
                for t in range(TT):
                    sq = act.activation(junk[:, t * D:(t + 1) * D], xin[:, t, :], ACT.Square, accum_out=ss[:, t:t + 1])
                sq.then_inc(squares_ready, 1)

            def normalise(b):
                act.wait_ge(rstd_ready, b + 1)
                for t in range(TT):
                    act.activation(xin[:, t, :], xin[:, t, :], ACT.Copy, scale=rstd[:, t:t + 1])\
                       .then_inc(xn_ready, 1)

            def x_high(b, k):
                act.wait_ge(xT_psum, KT * b + (k + 1))
                act.activation(xT_tile(b, 0, k), X[:, :], ACT.Copy, scale=scl_of(b, k)).then_inc(xhi_ready, 1)

            def w_high(p):
                act.wait_ge(w_scale_ready, p + 1)
                if p >= 2:
                    act.wait_ge(wT_psum, VG * (p - 1))
                for v in (1, 0):
                    act.activation(whl[:, p % 2, v, 0:D], wst[:, p % WSTAGE, v, :], ACT.Copy,
                                   scale=inv_w[:, VG * p + v:VG * p + v + 1]).then_inc(whi_ready, 1)

            def w_out(p, v):
                n = VG * p + (1 - v)
                act.wait_ge(wT_psum, n + 1)
                act.activation(wT[:, p, v, :], WB[n % 3][:, :].bitcast(F16), ACT.Copy).then_inc(wT_ready, 1)

            def gelu(b, s):
                act.wait_ge(gate_ready, FT * b + (s + 1))
                if not isinstance(b, int) or b > 0 or s >= 2:
                    act.wait_ge(h_ready, FT * b + (s - 1))
                act.activation(g[:, s % 2, :], G[s % 2][:, :], ACT.Gelu, scale=c_of(b, s, 1))\
                   .then_inc(gelu_done, 1)

            squares(0)
            w_high(0)
            act.wait_ge(scl_ready, 1)
            normalise(0)
            w_out(0, 1)
            w_out(0, 0)
            for k in range(KT):
                x_high(0, k)
            for s in range(FT):
                if s + 1 < FT:
                    w_high(s + 1)
                    w_out(s + 1, 1)
                act.wait_ge(c_ready, s + 1)
                gelu(0, s)
                if s + 1 < FT:
                    w_out(s + 1, 0)
                if s == 1:
                    squares(1)
                if s == 3:
                    normalise(1)
                if s in XPREP_AT:
                    x_high(1, XPREP_AT[s])
                if s in DW_SUM:
                    k = DW_SUM[s]
                    act.wait_ge(dw_loaded[k], 16)
                    if k > 0:
                        act.wait_ge(dw_sums, k)
                    act.activation(junk[:, :], dw[k], ACT.Abs, accum_out=dwsum[:, k:k + 1]).then_inc(dw_sums, 1)
            act.wait_ge(c_ready, FT + 1)
            with act.Fori(1, LAST) as b:
                for s in range(FT):
                    gelu(b, s)
                    if s == 0:
                        squares(b + 1)
                    if s == 3:
                        normalise(b + 1)
                    if s in XPREP_AT:
                        x_high(b + 1, XPREP_AT[s])
            for s in range(FT):
                gelu(LAST, s)

        @block.vector
        def _(dve):
            def rms(b):
                dve.wait_ge(squares_ready, b + 1)
                dve.tensor_scalar(ms[:, :], ss[:, :], 1.0 / D, RMS_EPS, ALU.mult, ALU.add).then_inc(ms_ready, 1)

            def refine(b):
                dve.wait_ge(pow_ready, b + 1)
                dve.tensor_tensor(r_a[:, :], r_pow[:, :], r_pow[:, :], ALU.mult).then_inc(newton_steps, 1)
                dve.wait_ge(newton_steps, 3 * b + 1)
                dve.tensor_tensor(r_b[:, :], r_a[:, :], ms[:, :], ALU.mult).then_inc(newton_steps, 1)
                dve.wait_ge(newton_steps, 3 * b + 2)
                dve.tensor_scalar(r_a[:, :], r_b[:, :], -0.5, 1.5, ALU.mult, ALU.add).then_inc(newton_steps, 1)
                dve.wait_ge(newton_steps, 3 * b + 3)
                dve.tensor_tensor(rstd[:, :], r_pow[:, :], r_a[:, :], ALU.mult).then_inc(rstd_ready, 1)

            def x_low(b, k):
                dve.wait_ge(xhi_ready, KT * b + (k + 1))
                dve.scalar_tensor_tensor(out=xT_tile(b, 1, k), in0=X[:, :], scalar=scl_of(b, k),
                                         in1=xT_tile(b, 0, k), op0=ALU.mult, op1=ALU.subtract)\
                   .then_inc(xlo_ready, 1)

            def w_scale(p):
                pair = slice(VG * p, VG * p + VG)
                dve.wait_ge(w_loaded[p % WSTAGE], 16 * (p // WSTAGE + 1))
                dve.tensor_reduce(inv_w[:, pair], wst[:, p % WSTAGE, :, :], AX.X, ALU.max,
                                  apply_absolute_value=True).then_inc(w_steps, 1)
                dve.wait_ge(w_steps, 3 * p + 1)
                dve.tensor_scalar(c_w[:, pair], inv_w[:, pair], TINY, 1.0 / W_GAIN, ALU.max, ALU.mult)\
                   .then_inc(w_steps, 1)
                dve.wait_ge(w_steps, 3 * p + 2)
                dve.tensor_scalar(c_w[:, pair].bitcast(I32), c_w[:, pair].bitcast(I32), EXPONENT, None,
                                  ALU.bitwise_and).then_inc(w_steps, 1)
                dve.wait_ge(w_steps, 3 * p + 3)
                dve.reciprocal(inv_w[:, pair], c_w[:, pair]).then_inc(w_scale_ready, 1)

            def w_low(p):
                for i, v in enumerate((1, 0)):
                    dve.wait_ge(whi_ready, VG * p + i + 1)
                    dve.scalar_tensor_tensor(out=whl[:, p % 2, v, D:2 * D], in0=wst[:, p % WSTAGE, v, :],
                                             scalar=inv_w[:, VG * p + v:VG * p + v + 1],
                                             in1=whl[:, p % 2, v, 0:D], op0=ALU.mult, op1=ALU.subtract)\
                       .then_inc(wlo_ready, 1)

            def c_first(p):
                pair = slice(VG * p, VG * p + VG)
                dve.tensor_scalar(c_all[:, pair], c_w[:, pair], c_b[:, 0:1], None, ALU.mult).then_inc(c_ready, 1)

            def hidden(b, s):
                n = FT * b + (s + 1)
                dve.wait_ge(val_ready, n)
                dve.wait_ge(gelu_done, n)
                dve.scalar_tensor_tensor(out=h_tiles(b, s, 1), in0=V[s % 2][:, :], scalar=c_of(b, s, 0),
                                         in1=g[:, s % 2, :], op0=ALU.mult, op1=ALU.mult).then_inc(h_ready, 1)

            def largest(b, j):
                s, n = MAX_GROUPS[j]
                done = MAX_OPS * b + 2 * j
                into = mpart if j > 0 else m
                dve.wait_ge(h_ready, FT * b + (s + n))
                if j == 0 and not (isinstance(b, int) and b == 0):
                    dve.wait_ge(amaxT_psum, b)
                    dve.memset(mpart[:, 0:1], 0.0)
                dve.tensor_reduce(into[:, :], h_tiles(b, s, n).rearrange("p (j t) -> p t j", t=T), AX.X, ALU.max,
                                  apply_absolute_value=True).then_inc(max_ready, 1)
                if j > 0:
                    dve.wait_ge(max_ready, done)
                    dve.tensor_tensor(m[:, :], m[:, :], mpart[:, :], ALU.max).then_inc(max_ready, 1)

            def quant_scale(b):
                dve.wait_ge(amaxT_psum, b + 1)
                dve.tensor_reduce(qscale[:, :], X[:, :].rearrange("p (t f) -> p t f", t=TT), AX.X, ALU.max)\
                   .then_inc(amax_steps, 1)
                dve.wait_ge(amax_steps, 3 * b + 1)
                dve.tensor_scalar(amax[:, :], qscale[:, :], QEPS, None, ALU.max).then_inc(amax_steps, 1)
                dve.wait_ge(amax_steps, 3 * b + 2)
                dve.reciprocal(amax_inv[:, :], amax[:, :]).then_inc(amax_steps, 1)
                dve.wait_ge(amax_steps, 3 * b + 3)
                dve.tensor_scalar(qscale[:, :], amax_inv[:, :], QMAX, None, ALU.mult).then_inc(qscale_ready, 1)
                dve.tensor_scalar(dq[:, :], amax[:, :], mdq[:, 0:1], None, ALU.mult).then_inc(dq_ready, 1)

            def quantise(b, i):
                s = 2 * PAIR_ORDER[i]
                n = PAIRS * b + (i + 1)
                pair = h_tiles(b, s, 2)
                dve.wait_ge(qscale_psum, b + 1)
                dve.tensor_tensor(pair.rearrange("p (a t) -> p a t", a=2), pair.rearrange("p (a t) -> p a t", a=2),
                                  S[:, :].unsqueeze(1).to_broadcast([P, 2, T]), ALU.mult).then_inc(q_scaled, 1)
                dve.wait_ge(q_scaled, n)
                dve.tensor_scalar(pair, pair, QMAX, QMIN, ALU.min, ALU.max).then_inc(q_clipped, 1)
                dve.wait_ge(q_clipped, n)
                dve.tensor_scalar(q[:, s * T:(s + 2) * T], pair, MAGIC, MAGIC, ALU.add, ALU.subtract)\
                   .then_inc(q_ready, 1)

            def y_out(b, t, bank):
                dve.wait_ge(dq_ready, b + 1)
                dve.wait_ge(y_psum, TT * b + (t + 1))
                dve.wait_ge(xres_loaded[t % 2], 32 * b + 16 * (t // 2 + 1))
                dve.wait_ge(ystage_free[t % 2], 32 * b + 16 * (t // 2 + 1))
                dve.scalar_tensor_tensor(out=ystage[:, t % 2, :], in0=bank[:, :], scalar=dq[:, t:t + 1],
                                         in1=xres[:, t % 2, :], op0=ALU.mult, op1=ALU.add).then_inc(y_done, 1)

            for i in range(2):
                dve.memset(dq[:, i:i + 1], 0.0).then_inc(ystage_free[i], 16)

            w_scale(0)
            dve.wait_ge(condT_psum, 1)
            dve.tensor_copy(nwT, G[0][:, :].rearrange("p (k c) -> p k c", k=KT))
            dve.tensor_copy(cndT, V[0][:, 0:B]).then_inc(condT_ready, 1)
            dve.wait_ge(scl_psum, 1)
            dve.tensor_scalar(scl[:, :], G[1][:, 0:KT * B], 1.0, None, ALU.add).then_inc(scl_steps, 1)
            dve.wait_ge(scl_steps, 1)
            dve.tensor_reduce(bmax[:, :], scl[:, :].rearrange("p (k b) -> p b k", b=B), AX.X, ALU.max,
                              apply_absolute_value=True).then_inc(scl_steps, 1)
            rms(0)
            w_low(0)
            dve.wait_ge(bmaxT_psum, 1)
            dve.tensor_reduce(brow[:, :], V[1][0:B, 0:P], AX.X, ALU.max).then_inc(scl_steps, 1)
            refine(0)
            dve.wait_ge(bmax_psum, 1)
            dve.tensor_scalar(c_b[:, :], V[0][:, 0:B], TINY, 1.0 / H_GAIN, ALU.max, ALU.mult).then_inc(scl_steps, 1)
            dve.wait_ge(scl_steps, 4)
            dve.tensor_scalar(c_b[:, :].bitcast(I32), c_b[:, :].bitcast(I32), EXPONENT, None, ALU.bitwise_and)\
               .then_inc(scl_steps, 1)
            dve.wait_ge(scl_steps, 5)
            dve.reciprocal(inv_b[:, :], c_b[:, :]).then_inc(scl_steps, 1)
            dve.wait_ge(scl_steps, 6)
            dve.tensor_tensor(scl[:, :].rearrange("p (k b) -> p k b", b=B), scl[:, :].rearrange("p (k b) -> p k b", b=B),
                              inv_b[:, :].unsqueeze(1).to_broadcast([P, KT, B]), ALU.mult).then_inc(scl_ready, 1)
            dve.wait_ge(scl_ready, 1)
            c_first(0)
            w_scale(1)
            for k in range(KT):
                x_low(0, k)

            def down_weights(s):
                if s == DW_TOTAL:
                    dve.wait_ge(dw_total_psum, 1)
                    dve.tensor_reduce(dwmean[:, :], X[:, 0:KT], AX.X, ALU.add).then_inc(dw_steps, 1)
                    dve.wait_ge(dw_steps, 1)
                    dve.tensor_scalar(dwmean[:, :], dwmean[:, :], 1.0 / (D * FF), QEPS, ALU.mult, ALU.max)\
                       .then_inc(dw_steps, 1)
                    dve.wait_ge(dw_steps, 2)
                    dve.reciprocal(sw[:, :], dwmean[:, :]).then_inc(dw_scale_ready, 1)
                    dve.tensor_scalar(mdq[:, :], dwmean[:, :], 1.0 / QMAX, None, ALU.mult).then_inc(dw_steps, 1)
                if s in DW_TERN:
                    k = DW_TERN[s]
                    dve.wait_ge(dw_clipped, k + 1)
                    if k > 0:
                        dve.wait_ge(dT_psum, 2 * k)
                    dve.tensor_scalar(tern, dw[k], MAGIC, MAGIC, ALU.add, ALU.subtract).then_inc(dw_rounded, 1)

            def down_weights_out(s):
                if s in DW_T:
                    k = DW_T[s]
                    for half in range(2):
                        dve.wait_ge(dT_psum, 2 * k + half + 1)
                        dve.tensor_copy(dT[:, half * PAIRS:(half + 1) * PAIRS, k * P:(k + 1) * P],
                                        X[:, :].bitcast(F16).rearrange("p (f d) -> p f d", d=P)).then_inc(dT_ready, 1)

            for s in range(FT):
                if s + 1 < FT:
                    w_low(s + 1)
                if s + 2 < FT:
                    w_scale(s + 2)
                if s + 1 < FT:
                    c_first(s + 1)
                hidden(0, s)
                if s in MAX_AFTER:
                    largest(0, MAX_AFTER[s])
                if s == 1:
                    rms(1)
                if s == 2:
                    refine(1)
                if s in XPREP_AT:
                    x_low(1, XPREP_AT[s])
                down_weights_out(s)
                down_weights(s)
            dve.wait_ge(gelu_done, FT)
            dve.tensor_tensor(c_all[:, :].rearrange("p (b n) -> p b n", b=B),
                              c_w[:, :].unsqueeze(1).to_broadcast([P, B, FT * VG]),
                              c_b[:, :].unsqueeze(2).to_broadcast([P, B, FT * VG]), ALU.mult).then_inc(c_ready, 1)
            dve.wait_ge(c_ready, FT + 1)

            def behind(b, s):
                if QUANT_FROM <= s < QUANT_FROM + PAIRS:
                    quantise(b - 1, s - QUANT_FROM)
                if s - 1 in DOWN_AFTER:
                    t = DOWN_AFTER[s - 1]
                    y_out(b - 1, t, Y[t % 2])

            with dve.Fori(1, LAST) as b:
                for s in range(FT):
                    if s == 0:
                        quant_scale(b - 1)
                    hidden(b, s)
                    if s in MAX_AFTER:
                        largest(b, MAX_AFTER[s])
                    if s == 1:
                        rms(b + 1)
                    if s == 2:
                        refine(b + 1)
                    if s in XPREP_AT:
                        x_low(b + 1, XPREP_AT[s])
                    behind(b, s)
            for s in range(FT):
                if s == 0:
                    quant_scale(LAST - 1)
                hidden(LAST, s)
                if s in MAX_AFTER:
                    largest(LAST, MAX_AFTER[s])
                behind(LAST, s)
            quant_scale(LAST)
            for i in range(PAIRS):
                quantise(LAST, i)
            for t in range(TT):
                y_out(LAST, t, TAIL[t])

        @block.tensor
        def _(pe):
            def transpose_x(b, k):
                if k == 0:
                    pe.wait_ge(xn_ready, TT * b + TT)
                if not isinstance(b, int) or b > 0 or k > 0:
                    pe.wait_ge(xlo_ready, KT * b + k)
                for t in range(TT):
                    tr = pe.transpose(X[:, t * P:(t + 1) * P], xin[:, t, k * P:(k + 1) * P], ident[:, :])
                tr.then_inc(xT_psum, 1)

            def transpose_w(p, v):
                n = VG * p + (1 - v)
                pe.wait_ge(wlo_ready, n + 1)
                if n >= 3:
                    pe.wait_ge(wT_ready, n - 2)
                bank = WB[n % 3][:, :].bitcast(F16)
                for j in range(2 * KT):
                    tr = pe.transpose(bank[:, j * P:(j + 1) * P], whl[:, p % 2, v, j * P:(j + 1) * P], ident16[:, :])
                tr.then_inc(wT_psum, 1)

            def transpose_dw(k, half):
                pe.wait_ge(dw_rounded, k + 1)
                if k > 0 or half > 0:
                    pe.wait_ge(dT_ready, 2 * k + half)
                for j in range(PAIRS):
                    tr = pe.transpose(X[:, :].bitcast(F16)[:, j * P:(j + 1) * P],
                                      tern[:, (half * PAIRS + j) * P:(half * PAIRS + j + 1) * P], ident16[:, :])
                tr.then_inc(dT_psum, 1)

            def up(b, s, v):
                n = FT * b + (s - 1)
                bank, done, free = (G[s % 2], gate_ready, gelu_done) if v else (V[s % 2], val_ready, h_ready)
                if not isinstance(b, int) or b > 0 or s >= 2:
                    pe.wait_ge(free, n)
                for k in range(KT):
                    high = wT[:, s, v, k * P:(k + 1) * P]
                    low = wT[:, s, v, (KT + k) * P:(KT + k + 1) * P]
                    pe.matmul(bank[:, :], high, xT_tile(b, 0, k), start=(k == 0), stop=False)
                    pe.matmul(bank[:, :], high, xT_tile(b, 1, k), start=False, stop=False)
                    mm = pe.matmul(bank[:, :], low, xT_tile(b, 0, k), start=False, stop=(k == KT - 1))
                mm.then_inc(done, 1)

            def transpose_max(b):
                pe.wait_ge(max_ready, MAX_OPS * b + MAX_OPS)
                pe.wait_ge(xlo_ready, KT * b + KT)
                for t in range(TT):
                    tr = pe.transpose(X[:, t * P:(t + 1) * P], m[:, t * P:(t + 1) * P], ident[:, :])
                tr.then_inc(amaxT_psum, 1)

            def spread_scale(b):
                pe.wait_ge(qscale_ready, b + 1)
                for t in range(TT):
                    tr = pe.transpose(S[:, t * P:(t + 1) * P], qscale[:, t:t + 1].to_broadcast([P, P]), ident[:, :])
                tr.then_inc(qscale_psum, 1)

            def down(b, t):
                pe.wait_ge(q_ready, PAIRS * b + PAIRS)
                if t >= 2:
                    pe.wait_ge(y_done, TT * b + (t - 1))
                for s in range(FT):
                    mm = pe.matmul(Y[t % 2][:, :], q[:, s * T + t * P:s * T + (t + 1) * P], dT[:, s, :],
                                   start=(s == 0), stop=(s == FT - 1))
                mm.then_inc(y_psum, 1)

            pe.wait_ge(consts_ready, 1)
            pe.wait_ge(cond_loaded, 32)
            for k in range(KT):
                pe.transpose(G[0][:, k * P:(k + 1) * P], nw[:, k, :], ident[:, :])
            pe.transpose(V[0][:, 0:B], cnd, ident[0:B, 0:B]).then_inc(condT_psum, 1)
            pe.wait_ge(condT_ready, 1)
            for k in range(KT):
                mm = pe.matmul(G[1][:, k * B:(k + 1) * B], nwT[:, k, :], cndT, start=True, stop=True)
            mm.then_inc(scl_psum, 1)
            pe.wait_ge(scl_steps, 2)
            pe.transpose(V[1][0:B, 0:P], bmax[:, :], ident[:, :]).then_inc(bmaxT_psum, 1)
            transpose_w(0, 1)
            transpose_w(0, 0)
            pe.wait_ge(scl_steps, 3)
            pe.transpose(V[0][:, 0:B], brow[:, :].to_broadcast([B, P]), ident[0:B, 0:B]).then_inc(bmax_psum, 1)
            for k in range(KT):
                transpose_x(0, k)
            pe.wait_ge(xlo_ready, KT)
            for s in range(FT):
                for v in (1, 0):
                    pe.wait_ge(wT_ready, VG * s + 2 - v)
                    up(0, s, v)
                    if s + 1 < FT:
                        transpose_w(s + 1, v)
                    if s in DW_T:
                        transpose_dw(DW_T[s], 1 - v)
                if s in XPREP_AT:
                    transpose_x(1, XPREP_AT[s])
                if s == DW_TOTAL - 1:
                    pe.wait_ge(dw_sums, KT)
                    pe.matmul(X[:, 0:KT], ones[:, :], dwsum[:, :], start=True, stop=True).then_inc(dw_total_psum, 1)
            pe.wait_ge(wT_ready, VG * FT)
            pe.wait_ge(dT_ready, 2 * KT)

            def behind(b, s):
                if s == 0:
                    spread_scale(b - 1)
                if s in DOWN_AFTER:
                    down(b - 1, DOWN_AFTER[s])

            with pe.Fori(1, LAST) as b:
                for s in range(FT):
                    if s == 0:
                        pe.wait_ge(xlo_ready, KT * b + KT)
                    up(b, s, 1)
                    if s == 0:
                        transpose_max(b - 1)
                    up(b, s, 0)
                    if s in XPREP_AT:
                        transpose_x(b + 1, XPREP_AT[s])
                    behind(b, s)
            pe.wait_ge(xlo_ready, KT * B)
            for s in range(FT):
                up(LAST, s, 1)
                if s == 0:
                    transpose_max(LAST - 1)
                up(LAST, s, 0)
                behind(LAST, s)
            transpose_max(LAST)
            spread_scale(LAST)
            for i in range(PAIRS):
                pe.wait_ge(q_ready, PAIRS * LAST + i + 1)
                for s in (2 * PAIR_ORDER[i], 2 * PAIR_ORDER[i] + 1):
                    for t in range(TT):
                        mm = pe.matmul(TAIL[t][:, :], q[:, s * T + t * P:s * T + (t + 1) * P], dT[:, s, :],
                                       start=(s == 2 * PAIR_ORDER[0]), stop=(s == 2 * PAIR_ORDER[-1] + 1))
                        if s == 2 * PAIR_ORDER[-1] + 1:
                            mm.then_inc(y_psum, 1)


_INS = ["x", "cond_256", "L0_cond_norm_w", "L0_cond_up_w", "L0_cond_down_w"]
_OUTS = [((8, 512, 512), "float32")]


def kernel(**inputs):
    import numpy as _np
    import concourse.bacc as _bacc
    from concourse import mybir as _mybir
    from concourse.bass_utils import run_bass_kernel_spmd as _run

    nc = _bacc.Bacc("TRN2", target_bir_lowering=False, num_devices=1)
    arrays, args = {}, []
    for name in _INS:
        a = _np.ascontiguousarray(inputs[name])
        arrays[f"in_{name}_dram"] = a
        args.append(nc.dram_tensor(f"in_{name}_dram", a.shape, _mybir.dt.from_np(a.dtype), kind="ExternalInput").ap())
    for i, (shape, dtype) in enumerate(_OUTS):
        dt = _mybir.dt.from_np(_np.dtype(dtype))
        args.append(nc.dram_tensor(f"out_{i}_dram", shape, dt, kind="ExternalOutput").ap())
    gated_ffn_program(nc, *args)
    r = _run(nc, [arrays], core_ids=[0])
    return r.results[0]["out_0_dram"]
```

```python
import concourse.bass as bass
from concourse import mybir
from contextlib import ExitStack


def gated_ffn_program(nc, x, cond, norm_w, up_w, down_w, out):
    F32, F16, I32 = mybir.dt.float32, mybir.dt.float16, mybir.dt.int32
    ALU, ACT, AX = mybir.AluOpType, mybir.ActivationFunctionType, mybir.AxisListType

    P = nc.NUM_PARTITIONS
    B, T, D = x.shape
    C = cond.shape[1]
    FF = down_w.shape[1]
    KT = D // P
    TT = T // P
    FT = FF // P
    VG = 2
    LAST = B - 1

    MAGIC = 1.5 * 2.0 ** 23
    EXPONENT = 0x7F800000
    TINY = 2.0 ** -100
    W_GAIN = 2.0 ** 13
    H_GAIN = 2.0 ** 9
    RMS_EPS = 1e-6
    QMAX, QMIN, QEPS = 127.0, -128.0, 1e-5

    EARLY = 4
    PAIRS = FT // 2
    QUANT_FROM = 0
    PAIR_ORDER = [(EARLY // 2 + i) % PAIRS for i in range(PAIRS)]
    XPREP_AT = {4 + k: k for k in range(KT)}
    DOWN_AFTER = {9: 0, 11: 1, 13: 2, 14: 3}
    DOWN_AFTER_IN_A = {11: 0, 12: 1, 13: 2, 14: 3}
    DOWN_AFTER_IN_B = {9: 0, 11: 1}
    MAX_GROUPS = [(0, 4), (4, 4), (8, 4), (12, 3), (15, 1)]
    MAX_OPS = 2 * len(MAX_GROUPS) - 1
    MAX_AFTER = {s + n - 1: j for j, (s, n) in enumerate(MAX_GROUPS)}
    WSTAGE = 3
    SQUARES_0 = {1: (0, 1), 2: (2, 3)}
    RMS_0, NORMALISE_0 = 3, 4
    XPREP_AT_0 = {5 + k: k for k in range(KT)}
    DW_LOAD = {k: k for k in range(KT)}
    DW_SUM = {2 + k: k for k in range(KT)}
    DW_TOTAL = 6
    DW_SCALE = {7: 0, 9: 1, 11: 2, 12: 3}
    DW_ROUND = {8: 0, 10: 1, 12: 2, 14: 3}
    DW_T = {9: 0, 11: 1, 13: 2, 15: 3}

    x_v = x.rearrange("b (t p) d -> b p t d", p=P)
    out_v = out.rearrange("b (t p) d -> b p t d", p=P)
    up_v = up_w.rearrange("(v s p) d -> s p v d", v=VG, p=P)
    dw_v = down_w.rearrange("(k p) f -> k p f", p=P)

    ctx = ExitStack()
    with ctx:
        def sb(name, shape, dt):
            return ctx.enter_context(nc.sbuf_tensor(name, shape, dt))

        def pb(name):
            return ctx.enter_context(nc.psum_tensor(name, [P, 512], F32))

        def sem(name):
            return ctx.enter_context(nc.semaphore(name))

        wT = sb("wT", [P, FT, VG, 2 * KT * P], F16)
        dT = sb("dT", [P, FT, D], F16)
        h = sb("h", [P, (FT + EARLY) * T], F32)
        q = sb("q", [P, FT * T], F16)
        xT = sb("xT", [P, 2 * 2 * KT * T], F16)
        xin = sb("xin", [P, TT, D], F32)
        xres = sb("xres", [P, 2, D], F32)
        g = sb("g", [P, 2, T], F32)
        m = sb("m", [P, T], F32)
        mpart = sb("mpart", [P, T], F32)
        junk = sb("junk", [P, FF], F16)
        ident = sb("ident", [P, P], F32)
        ident16 = sb("ident16", [P, P], F16)
        ones = sb("ones", [P, P], F32)
        c_w = sb("c_w", [P, FT * VG], F32)
        inv_w = sb("inv_w", [P, FT * VG], F32)
        c_all = sb("c_all", [P, B * FT * VG], F32)
        c_b = sb("c_b", [P, B], F32)
        inv_b = sb("inv_b", [P, B], F32)
        scl = sb("scl", [P, KT * B], F32)
        bmax = sb("bmax", [P, B], F32)
        brow = sb("brow", [B, 1], F32)
        ss, ms, neg_half, r_pow, r_a, r_b, rstd, amax, amax_inv, qscale, dq = [
            sb(n, [P, TT], F32) for n in
            "ss ms neg_half r_pow r_a r_b rstd amax amax_inv qscale dq".split()]
        dwsum = sb("dwsum", [P, KT], F32)
        dwmean, sw, mdq = [sb(n, [P, 1], F32) for n in ("dwmean", "sw", "mdq")]

        wst = sb("wst", [P, WSTAGE, VG, D], F32)
        whl = sb("whl", [P, 2, VG, 2 * D], F16)
        ystage = whl[:, 0, :, :].rearrange("p v n -> p (v n)").bitcast(F32).rearrange("p (a d) -> p a d", a=2)
        dw2 = sb("dw2", [P, FF], F32)
        q32 = q[:, :].bitcast(F32)
        dw = [q32[:, 0:FF], q32[:, FF:2 * FF], dw2[:, :], h[:, FT * T:(FT + EARLY) * T]]
        ytail = wst[:, :, :, :].rearrange("p a v d -> p (a v) d")[:, 0:TT, :]
        tern = xres[:, :, :].rearrange("p a d -> p (a d)").bitcast(F16)
        nw = h[:, (FT - 1) * T:FT * T].rearrange("p (k c) -> p k c", k=KT)
        nwT = h[:, (FT - 2) * T:(FT - 1) * T].rearrange("p (k c) -> p k c", k=KT)
        cnd = h[0:B, (FT - 3) * T:(FT - 3) * T + C]
        cndT = h[:, (FT - 4) * T:(FT - 4) * T + B]

        class Unit:
            def __init__(self, b, i, t, n):
                self.b, self.i, self.tiles, self.cols = b, i, range(t, t + n), slice(t * P, (t + n) * P)
                self.first = isinstance(i, int) and i == 0

        def whole(b):
            return Unit(b, b, 0, TT)

        def down_after(prev):
            if isinstance(prev.i, int):
                return DOWN_AFTER_IN_B if prev is HALF_A else DOWN_AFTER_IN_A
            return DOWN_AFTER

        HALF_A = Unit(LAST, LAST, 0, TT // 2)
        HALF_B = Unit(LAST, LAST + 1, TT // 2, TT // 2)

        def dw_out(k, half):
            return dT[:, half * PAIRS:(half + 1) * PAIRS, k * P:(k + 1) * P], \
                X[:, :].bitcast(F16).rearrange("p (f d) -> p f d", d=P)

        def h_tiles(u, s, n):
            at = s * T + (u.b % 2 * FT * T if s < EARLY else 0)
            return h[:, bass.ds(at, n * T)].rearrange("p (n t) -> p n t", t=T)[:, :, u.cols]

        def xT_tile(b, part, k, cols=slice(0, T)):
            at = b % 2 * (2 * KT * T) + ((part * KT + k) * T + cols.start)
            return xT[:, bass.ds(at, cols.stop - cols.start)]

        def c_of(b, s, v):
            return c_all[:, bass.ds(b * (FT * VG) + (s * VG + v), 1)]

        def scl_of(b, k):
            return scl[:, bass.ds(b + k * B, 1)]

        def x_block(ap, b):
            return ap[b] if isinstance(b, int) else ap[bass.ds(b, 1)].rearrange("o p t d -> p (o t) d")

        def x_tile(ap, b, t):
            return ap[b, :, t, :] if isinstance(b, int) else ap[bass.ds(b, 1), :, t, :].rearrange("o p d -> p (o d)")

        V = [pb("V0"), pb("V1")]
        G = [pb("G0"), pb("G1")]
        X = pb("X")
        S = pb("S")
        Y = [pb("Y0"), pb("Y1")]
        WB = [S, Y[0], Y[1]]
        X0 = [X, V[1], G[1], Y[1]]

        consts_ready = sem("consts_ready")
        ident_steps = sem("ident_steps")
        cond_loaded = sem("cond_loaded")
        norm_w_loaded = sem("norm_w_loaded")
        condT_psum = sem("condT_psum")
        condT_ready = sem("condT_ready")
        scl_psum = sem("scl_psum")
        scl_steps = sem("scl_steps")
        bmaxT_psum = sem("bmaxT_psum")
        bmax_psum = sem("bmax_psum")
        scl_ready = sem("scl_ready")
        x0_loaded = [sem(f"x0_loaded{t}") for t in range(TT)]
        x_loaded = sem("x_loaded")
        squares_ready = sem("squares_ready")
        ms_ready = sem("ms_ready")
        pow_ready = sem("pow_ready")
        newton_steps = sem("newton_steps")
        rstd_ready = sem("rstd_ready")
        xn_ready = sem("xn_ready")
        xT_psum = sem("xT_psum")
        xhi_ready = sem("xhi_ready")
        xlo_ready = sem("xlo_ready")
        w_loaded = [sem(f"w_loaded{i}") for i in range(WSTAGE)]
        w_steps = sem("w_steps")
        w_scale_ready = sem("w_scale_ready")
        whi_ready = sem("whi_ready")
        wlo_ready = sem("wlo_ready")
        wT_psum = sem("wT_psum")
        wT_ready = sem("wT_ready")
        c_ready = sem("c_ready")
        dw_loaded = [sem(f"dw_loaded{i}") for i in range(KT)]
        dw_sums = sem("dw_sums")
        dw_total_psum = sem("dw_total_psum")
        dw_steps = sem("dw_steps")
        dw_scale_ready = sem("dw_scale_ready")
        dw_scaled = sem("dw_scaled")
        dw_clipped = sem("dw_clipped")
        dw_rounded = sem("dw_rounded")
        dT_psum = sem("dT_psum")
        dT_ready = sem("dT_ready")
        gate_ready = sem("gate_ready")
        val_ready = sem("val_ready")
        gelu_done = sem("gelu_done")
        h_ready = sem("h_ready")
        max_ready = sem("max_ready")
        amaxT_psum = sem("amaxT_psum")
        amax_steps = sem("amax_steps")
        qscale_ready = sem("qscale_ready")
        dq_ready = sem("dq_ready")
        qscale_psum = sem("qscale_psum")
        q_scaled = sem("q_scaled")
        q_clipped = sem("q_clipped")
        q_ready = sem("q_ready")
        y_psum = sem("y_psum")
        y_done = sem("y_done")
        xres_loaded = [sem(f"xres_loaded{i}") for i in range(2)]
        ystage_free = [sem(f"ystage_free{i}") for i in range(2)]
        tail_stored = sem("tail_stored")

        block = ctx.enter_context(nc.Block())

        @block.sync
        def _(sp):
            def load_w(p):
                if p >= WSTAGE:
                    sp.wait_ge(wlo_ready, VG * (p - WSTAGE + 1))
                sp.dma_start(wst[:, p % WSTAGE], up_v[p]).then_inc(w_loaded[p % WSTAGE], 16)

            def load_x(b):
                sp.dma_start(xin[:, :, :], x_block(x_v, b)).then_inc(x_loaded, 16)

            def load_xres(b, t):
                sp.dma_start(xres[:, t % 2, :], x_tile(x_v, b, t)).then_inc(xres_loaded[t % 2], 16)

            def results(b):
                load_xres(b, 0)
                load_xres(b, 1)
                for t in range(TT):
                    sp.wait_ge(y_done, TT * b + (t + 1))
                    sp.dma_start(x_tile(out_v, b, t), ystage[:, t % 2, :]).then_inc(ystage_free[t % 2], 16)
                    if t + 2 < TT:
                        load_xres(b, t + 2)

            sp.dma_start(nw, norm_w.rearrange("(k p) c -> p k c", p=P)).then_inc(norm_w_loaded, 16)
            load_w(0)
            for t in range(TT):
                sp.dma_start(xin[:, t, :], x_tile(x_v, 0, t)).then_inc(x0_loaded[t], 16)
            for p in range(1, WSTAGE):
                load_w(p)
            sp.wait_ge(xT_psum, KT)
            load_x(1)
            for s in range(FT):
                if s + WSTAGE < FT:
                    load_w(s + WSTAGE)
                if s in DW_LOAD:
                    k = DW_LOAD[s]
                    sp.dma_start(dw[k], dw_v[k]).then_inc(dw_loaded[k], 16)
            sp.wait_ge(dT_psum, 2 * KT)
            with sp.Fori(1, LAST) as b:
                sp.wait_ge(xT_psum, KT * b + KT)
                load_x(b + 1)
                results(b - 1)
            sp.wait_ge(xT_psum, KT * B)
            load_x(LAST)
            results(LAST - 1)
            for t in range(TT):
                sp.wait_ge(y_done, TT * LAST + t + 1)
                sp.dma_start(out_v[LAST, :, t, :], ytail[:, t, :]).then_inc(tail_stored, 16)
            for i in range(2):
                sp.wait_ge(ystage_free[i], 16 + 16 * LAST * TT // 2)
            sp.wait_ge(tail_stored, 16 * TT)

        @block.gpsimd
        def _(pool):
            pool.memset(ident[:, :], 0.0).then_inc(ident_steps, 1)
            pool.memset(ones[:, :], 1.0)
            pool.memset(neg_half[:, :], -0.5)
            pool.wait_ge(ident_steps, 1)
            pool.affine_select(out=ident[:, :], in_=ident[:, :], compare_op=ALU.not_equal, fill=1.0,
                               base=0, pattern=[[-1, P]], channel_multiplier=1).then_inc(ident_steps, 1)
            pool.wait_ge(ident_steps, 2)
            pool.tensor_copy(ident16[:, :], ident[:, :]).then_inc(consts_ready, 1)

            def rsqrt(b):
                pool.wait_ge(ms_ready, b + 1)
                pool.tensor_tensor(r_pow[:, :], ms[:, :], neg_half[:, :], ALU.pow).then_inc(pow_ready, 1)

            rsqrt(0)
            with pool.Fori(1, B) as b:
                rsqrt(b)

        @block.scalar
        def _(act):
            act.dma_start(cnd, cond).then_inc(cond_loaded, 16)
            act.preload_act_table(ACT.Gelu)

            def squares(b, tiles=range(TT)):
                if isinstance(b, int) and b == 0:
                    pass
                else:
                    act.wait_ge(x_loaded, 16 * b)
                for t in tiles:
                    if isinstance(b, int) and b == 0:
                        act.wait_ge(x0_loaded[t], 16)
                    sq = act.activation(junk[:, t * D:(t + 1) * D], xin[:, t, :], ACT.Square, accum_out=ss[:, t:t + 1])
                if TT - 1 in tiles:
                    sq.then_inc(squares_ready, 1)

            def normalise(b):
                act.wait_ge(rstd_ready, b + 1)
                for t in range(TT):
                    act.activation(xin[:, t, :], xin[:, t, :], ACT.Copy, scale=rstd[:, t:t + 1])\
                       .then_inc(xn_ready, 1)

            def x_high(b, k, bank=X):
                act.wait_ge(xT_psum, KT * b + (k + 1))
                act.activation(xT_tile(b, 0, k), bank[:, :], ACT.Copy, scale=scl_of(b, k)).then_inc(xhi_ready, 1)

            def w_high(p):
                act.wait_ge(w_scale_ready, p + 1)
                if p >= 2:
                    act.wait_ge(wT_psum, VG * (p - 1))
                for v in (1, 0):
                    act.activation(whl[:, p % 2, v, 0:D], wst[:, p % WSTAGE, v, :], ACT.Copy,
                                   scale=inv_w[:, VG * p + v:VG * p + v + 1]).then_inc(whi_ready, 1)

            def w_out(p, v):
                n = VG * p + (1 - v)
                act.wait_ge(wT_psum, n + 1)
                act.activation(wT[:, p, v, :], WB[n % 3][:, :].bitcast(F16), ACT.Copy).then_inc(wT_ready, 1)

            def gelu(u, s):
                act.wait_ge(gate_ready, FT * u.i + (s + 1))
                if not u.first or s >= 2:
                    act.wait_ge(h_ready, FT * u.i + (s - 1))
                act.activation(g[:, s % 2, u.cols], G[s % 2][:, u.cols], ACT.Gelu, scale=c_of(u.b, s, 1))\
                   .then_inc(gelu_done, 1)

            squares(0)
            w_high(0)
            w_out(0, 1)
            act.wait_ge(scl_ready, 1)
            for k in range(KT):
                x_high(0, k, X0[k])
            w_out(0, 0)
            w_high(1)
            for s in range(FT):
                if 0 < s < FT - 2:
                    w_high(s + 2)
                act.wait_ge(c_ready, s + 1)
                gelu(whole(0), s)
                if s + 1 < FT:
                    w_out(s + 1, 1)
                if s == 0:
                    w_high(2)
                if s in SQUARES_0:
                    squares(1, SQUARES_0[s])
                if s in DW_SUM:
                    k = DW_SUM[s]
                    act.wait_ge(dw_loaded[k], 16)
                    if k == 0:
                        act.wait_ge(squares_ready, 2)
                    else:
                        act.wait_ge(dw_sums, k)
                    act.activation(junk[:, :], dw[k], ACT.Abs, accum_out=dwsum[:, k:k + 1]).then_inc(dw_sums, 1)
                if s in DW_SCALE:
                    k = DW_SCALE[s]
                    act.wait_ge(dw_scale_ready, 1)
                    act.activation(dw[k], dw[k], ACT.Copy, scale=sw[:, 0:1]).then_inc(dw_scaled, 1)
                if s + 1 < FT:
                    w_out(s + 1, 0)
                if s in DW_T:
                    n = 2 * DW_T[s] + 2
                    act.wait_ge(dT_psum, n)
                    act.activation(*dw_out(DW_T[s], 1), ACT.Copy).then_inc(dT_ready, 1)
                if s in XPREP_AT_0:
                    x_high(1, XPREP_AT_0[s])
            act.wait_ge(c_ready, FT + 1)
            with act.Fori(1, LAST) as b:
                for s in range(FT):
                    gelu(whole(b), s)
                    if s == 0:
                        squares(b + 1)
                    if s == 3:
                        normalise(b + 1)
                    if s in XPREP_AT:
                        x_high(b + 1, XPREP_AT[s])
            for u in (HALF_A, HALF_B):
                for s in range(FT):
                    gelu(u, s)

        @block.vector
        def _(dve):
            def rms(b):
                dve.wait_ge(squares_ready, b + 1)
                dve.tensor_scalar(ms[:, :], ss[:, :], 1.0 / D, RMS_EPS, ALU.mult, ALU.add).then_inc(ms_ready, 1)

            def refine(b):
                dve.wait_ge(pow_ready, b + 1)
                dve.tensor_tensor(r_a[:, :], r_pow[:, :], r_pow[:, :], ALU.mult).then_inc(newton_steps, 1)
                dve.wait_ge(newton_steps, 3 * b + 1)
                dve.tensor_tensor(r_b[:, :], r_a[:, :], ms[:, :], ALU.mult).then_inc(newton_steps, 1)
                dve.wait_ge(newton_steps, 3 * b + 2)
                dve.tensor_scalar(r_a[:, :], r_b[:, :], -0.5, 1.5, ALU.mult, ALU.add).then_inc(newton_steps, 1)
                dve.wait_ge(newton_steps, 3 * b + 3)
                dve.tensor_tensor(rstd[:, :], r_pow[:, :], r_a[:, :], ALU.mult).then_inc(rstd_ready, 1)

            def normalise(b):
                dve.wait_ge(rstd_ready, b + 1)
                for t in range(TT):
                    dve.tensor_scalar(xin[:, t, :], xin[:, t, :], rstd[:, t:t + 1], None, ALU.mult).then_inc(xn_ready, 1)

            def x_low(b, k, bank=X):
                dve.wait_ge(xhi_ready, KT * b + (k + 1))
                dve.scalar_tensor_tensor(out=xT_tile(b, 1, k), in0=bank[:, :], scalar=scl_of(b, k),
                                         in1=xT_tile(b, 0, k), op0=ALU.mult, op1=ALU.subtract)\
                   .then_inc(xlo_ready, 1)

            def w_scale(p):
                pair = slice(VG * p, VG * p + VG)
                dve.wait_ge(w_loaded[p % WSTAGE], 16 * (p // WSTAGE + 1))
                dve.tensor_reduce(inv_w[:, pair], wst[:, p % WSTAGE, :, :], AX.X, ALU.max,
                                  apply_absolute_value=True).then_inc(w_steps, 1)
                dve.wait_ge(w_steps, 3 * p + 1)
                dve.tensor_scalar(c_w[:, pair], inv_w[:, pair], TINY, 1.0 / W_GAIN, ALU.max, ALU.mult)\
                   .then_inc(w_steps, 1)
                dve.wait_ge(w_steps, 3 * p + 2)
                dve.tensor_scalar(c_w[:, pair].bitcast(I32), c_w[:, pair].bitcast(I32), EXPONENT, None,
                                  ALU.bitwise_and).then_inc(w_steps, 1)
                dve.wait_ge(w_steps, 3 * p + 3)
                dve.reciprocal(inv_w[:, pair], c_w[:, pair]).then_inc(w_scale_ready, 1)

            def w_low(p, parts=(1, 0)):
                for v in parts:
                    dve.wait_ge(whi_ready, VG * p + 2 - v)
                    dve.scalar_tensor_tensor(out=whl[:, p % 2, v, D:2 * D], in0=wst[:, p % WSTAGE, v, :],
                                             scalar=inv_w[:, VG * p + v:VG * p + v + 1],
                                             in1=whl[:, p % 2, v, 0:D], op0=ALU.mult, op1=ALU.subtract)\
                       .then_inc(wlo_ready, 1)

            def c_first(p):
                pair = slice(VG * p, VG * p + VG)
                dve.tensor_scalar(c_all[:, pair], c_w[:, pair], c_b[:, 0:1], None, ALU.mult).then_inc(c_ready, 1)

            def hidden(u, s):
                n = FT * u.i + (s + 1)
                dve.wait_ge(val_ready, n)
                dve.wait_ge(gelu_done, n)
                dve.scalar_tensor_tensor(out=h_tiles(u, s, 1).rearrange("p n t -> p (n t)"), in0=V[s % 2][:, u.cols],
                                         scalar=c_of(u.b, s, 0), in1=g[:, s % 2, u.cols],
                                         op0=ALU.mult, op1=ALU.mult).then_inc(h_ready, 1)
                if s in MAX_AFTER:
                    largest(u, MAX_AFTER[s])

            def largest(u, j):
                s, n = MAX_GROUPS[j]
                into = mpart if j > 0 else m
                dve.wait_ge(h_ready, FT * u.i + (s + n))
                if j == 0 and not u.first:
                    dve.wait_ge(amaxT_psum, u.i)
                    dve.memset(mpart[:, 0:1], 0.0)
                dve.tensor_reduce(into[:, u.cols], h_tiles(u, s, n).rearrange("p n t -> p t n"), AX.X, ALU.max,
                                  apply_absolute_value=True).then_inc(max_ready, 1)
                if j > 0:
                    dve.wait_ge(max_ready, MAX_OPS * u.i + 2 * j)
                    dve.tensor_tensor(m[:, u.cols], m[:, u.cols], mpart[:, u.cols], ALU.max).then_inc(max_ready, 1)

            def quant_scale(u):
                t = slice(u.tiles.start, u.tiles.stop)
                dve.wait_ge(amaxT_psum, u.i + 1)
                dve.tensor_reduce(qscale[:, t], X[:, u.cols].rearrange("p (t f) -> p t f", f=P), AX.X, ALU.max)\
                   .then_inc(amax_steps, 1)
                dve.wait_ge(amax_steps, 3 * u.i + 1)
                dve.tensor_scalar(amax[:, t], qscale[:, t], QEPS, None, ALU.max).then_inc(amax_steps, 1)
                dve.wait_ge(amax_steps, 3 * u.i + 2)
                dve.reciprocal(amax_inv[:, t], amax[:, t]).then_inc(amax_steps, 1)
                dve.wait_ge(amax_steps, 3 * u.i + 3)
                dve.tensor_scalar(qscale[:, t], amax_inv[:, t], QMAX, None, ALU.mult).then_inc(qscale_ready, 1)
                dve.tensor_scalar(dq[:, t], amax[:, t], mdq[:, 0:1], None, ALU.mult).then_inc(dq_ready, 1)

            def q_scale(u, i):
                pair = h_tiles(u, 2 * PAIR_ORDER[i], 2)
                dve.wait_ge(qscale_psum, u.i + 1)
                dve.tensor_tensor(pair, pair, S[:, u.cols].unsqueeze(1).to_broadcast([P, 2, len(u.tiles) * P]),
                                  ALU.mult).then_inc(q_scaled, 1)

            def q_clip(u, i):
                pair = h_tiles(u, 2 * PAIR_ORDER[i], 2)
                dve.wait_ge(q_scaled, PAIRS * u.i + (i + 1))
                dve.tensor_scalar(pair, pair, QMAX, QMIN, ALU.min, ALU.max).then_inc(q_clipped, 1)

            def q_round(u, i):
                s = 2 * PAIR_ORDER[i]
                dve.wait_ge(q_clipped, PAIRS * u.i + (i + 1))
                dve.tensor_scalar(q[:, s * T:(s + 2) * T].rearrange("p (n t) -> p n t", t=T)[:, :, u.cols],
                                  h_tiles(u, s, 2), MAGIC, MAGIC, ALU.add, ALU.subtract).then_inc(q_ready, 1)

            def y_out(u, t, bank, res, stage):
                dve.wait_ge(dq_ready, u.i + 1)
                dve.wait_ge(y_psum, TT * u.b + (t + 1))
                dve.scalar_tensor_tensor(out=stage, in0=bank[:, :], scalar=dq[:, t:t + 1], in1=res,
                                         op0=ALU.mult, op1=ALU.add).then_inc(y_done, 1)

            def behind(prev, s):
                if s < PAIRS:
                    q_scale(prev, s)
                    q_clip(prev, s)
                    q_round(prev, s)
                after = down_after(prev)
                if s - 1 in after:
                    t = after[s - 1]
                    if prev is HALF_A:
                        y_out(prev, t, Y[t % 2], xin[:, t, :], ytail[:, t, :])
                    else:
                        use = 32 * prev.b + 16 * (t // 2 + 1)
                        dve.wait_ge(xres_loaded[t % 2], use)
                        dve.wait_ge(ystage_free[t % 2], use)
                        y_out(prev, t, Y[t % 2], xres[:, t % 2, :], ystage[:, t % 2, :])

            for i in range(2):
                dve.memset(dq[:, i:i + 1], 0.0).then_inc(ystage_free[i], 16)

            dve.wait_ge(condT_psum, 1)
            dve.tensor_copy(nwT, G[0][:, :].rearrange("p (k c) -> p k c", k=KT))
            dve.tensor_copy(cndT, V[0][:, 0:B]).then_inc(condT_ready, 1)
            w_scale(0)
            dve.wait_ge(scl_psum, 1)
            dve.tensor_scalar(scl[:, :], G[1][:, 0:KT * B], 1.0, None, ALU.add).then_inc(scl_steps, 1)
            dve.wait_ge(scl_steps, 1)
            dve.tensor_reduce(bmax[:, :], scl[:, :].rearrange("p (k b) -> p b k", b=B), AX.X, ALU.max,
                              apply_absolute_value=True).then_inc(scl_steps, 1)
            dve.wait_ge(bmaxT_psum, 1)
            dve.tensor_reduce(brow[:, :], V[1][0:B, 0:P], AX.X, ALU.max).then_inc(scl_steps, 1)
            rms(0)
            dve.wait_ge(bmax_psum, 1)
            dve.tensor_scalar(c_b[:, :], V[0][:, 0:B], TINY, 1.0 / H_GAIN, ALU.max, ALU.mult).then_inc(scl_steps, 1)
            dve.wait_ge(scl_steps, 4)
            dve.tensor_scalar(c_b[:, :].bitcast(I32), c_b[:, :].bitcast(I32), EXPONENT, None, ALU.bitwise_and)\
               .then_inc(scl_steps, 1)
            dve.wait_ge(scl_steps, 5)
            dve.reciprocal(inv_b[:, :], c_b[:, :]).then_inc(scl_steps, 1)
            dve.wait_ge(scl_steps, 6)
            dve.tensor_tensor(scl[:, :].rearrange("p (k b) -> p k b", b=B), scl[:, :].rearrange("p (k b) -> p k b", b=B),
                              inv_b[:, :].unsqueeze(1).to_broadcast([P, KT, B]), ALU.mult).then_inc(scl_ready, 1)
            w_low(0, (1,))
            refine(0)
            normalise(0)
            w_low(0, (0,))
            dve.wait_ge(scl_ready, 1)
            c_first(0)
            w_scale(1)
            for k in range(KT):
                x_low(0, k, X0[k])
            w_low(1)
            w_scale(2)

            def down_mean():
                dve.wait_ge(dw_total_psum, 1)
                dve.tensor_reduce(dwmean[:, :], X[:, 0:KT], AX.X, ALU.add).then_inc(dw_steps, 1)
                dve.wait_ge(dw_steps, 1)
                dve.tensor_scalar(dwmean[:, :], dwmean[:, :], 1.0 / (D * FF), QEPS, ALU.mult, ALU.max)\
                   .then_inc(dw_steps, 1)
                dve.wait_ge(dw_steps, 2)
                dve.reciprocal(sw[:, :], dwmean[:, :]).then_inc(dw_scale_ready, 1)
                dve.tensor_scalar(mdq[:, :], dwmean[:, :], 1.0 / QMAX, None, ALU.mult).then_inc(dw_steps, 1)

            def down_round(k):
                dve.wait_ge(dw_scaled, k + 1)
                dve.tensor_scalar(dw[k], dw[k], 1.0, -1.0, ALU.min, ALU.max).then_inc(dw_clipped, 1)
                dve.wait_ge(dw_clipped, k + 1)
                if k > 0:
                    dve.wait_ge(dT_psum, 2 * k)
                dve.tensor_scalar(tern, dw[k], MAGIC, MAGIC, ALU.add, ALU.subtract).then_inc(dw_rounded, 1)

            for s in range(FT):
                if s + 2 < FT:
                    w_low(s + 2)
                if s + 3 < FT:
                    w_scale(s + 3)
                if s + 1 < FT:
                    c_first(s + 1)
                if s == DW_TOTAL:
                    down_mean()
                if s in DW_T:
                    dve.wait_ge(dT_psum, 2 * DW_T[s] + 1)
                    dve.tensor_copy(*dw_out(DW_T[s], 0)).then_inc(dT_ready, 1)
                if s in DW_ROUND:
                    down_round(DW_ROUND[s])
                hidden(whole(0), s)
                if s == RMS_0:
                    rms(1)
                if s == NORMALISE_0:
                    refine(1)
                    normalise(1)
                if s in XPREP_AT_0:
                    x_low(1, XPREP_AT_0[s])
            dve.wait_ge(gelu_done, FT)
            dve.tensor_tensor(c_all[:, :].rearrange("p (b n) -> p b n", b=B),
                              c_w[:, :].unsqueeze(1).to_broadcast([P, B, FT * VG]),
                              c_b[:, :].unsqueeze(2).to_broadcast([P, B, FT * VG]), ALU.mult).then_inc(c_ready, 1)
            dve.wait_ge(c_ready, FT + 1)
            with dve.Fori(1, LAST) as b:
                quant_scale(whole(b - 1))
                for s in range(FT):
                    hidden(whole(b), s)
                    if s == 1:
                        rms(b + 1)
                    if s == 2:
                        refine(b + 1)
                    if s in XPREP_AT:
                        x_low(b + 1, XPREP_AT[s])
                    behind(whole(b - 1), s)
            for prev, u in ((whole(LAST - 1), HALF_A), (HALF_A, HALF_B)):
                quant_scale(prev)
                if prev is HALF_A:
                    dve.wait_ge(x_loaded, 16 * B)
                for s in range(FT):
                    hidden(u, s)
                    behind(prev, s)
            quant_scale(HALF_B)
            for i in range(PAIRS + 1):
                if i < PAIRS:
                    q_scale(HALF_B, i)
                if i > 0:
                    q_round(HALF_B, i - 1)
                if i < PAIRS:
                    q_clip(HALF_B, i)
            for t in HALF_B.tiles:
                y_out(HALF_B, t, V[t % 2], xin[:, t, :], ytail[:, t, :])

        @block.tensor
        def _(pe):
            def transpose_x(b, k, bank=X):
                if k == 0:
                    pe.wait_ge(xn_ready, TT * b + TT)
                if bank is X and not (isinstance(b, int) and b == 0):
                    pe.wait_ge(xlo_ready, KT * b + k)
                for t in range(TT):
                    tr = pe.transpose(bank[:, t * P:(t + 1) * P], xin[:, t, k * P:(k + 1) * P], ident[:, :])
                tr.then_inc(xT_psum, 1)

            def transpose_w(p, v):
                n = VG * p + (1 - v)
                pe.wait_ge(wlo_ready, n + 1)
                if n >= 3:
                    pe.wait_ge(wT_ready, n - 2)
                bank = WB[n % 3][:, :].bitcast(F16)
                for j in range(2 * KT):
                    tr = pe.transpose(bank[:, j * P:(j + 1) * P], whl[:, p % 2, v, j * P:(j + 1) * P], ident16[:, :])
                tr.then_inc(wT_psum, 1)

            def transpose_dw(k, half):
                pe.wait_ge(dw_rounded, k + 1)
                if k == 0 and half == 0:
                    pe.wait_ge(xlo_ready, 2 * KT)
                else:
                    pe.wait_ge(dT_ready, 2 * k + half)
                for j in range(PAIRS):
                    tr = pe.transpose(X[:, :].bitcast(F16)[:, j * P:(j + 1) * P],
                                      tern[:, (half * PAIRS + j) * P:(half * PAIRS + j + 1) * P], ident16[:, :])
                tr.then_inc(dT_psum, 1)

            def up(u, s, v):
                bank, done, free = (G[s % 2], gate_ready, gelu_done) if v else (V[s % 2], val_ready, h_ready)
                if not u.first or s >= 2:
                    pe.wait_ge(free, FT * u.i + (s - 1))
                for k in range(KT):
                    if u.first and s == 0 and v:
                        pe.wait_ge(xlo_ready, k + 1)
                    high = wT[:, s, v, k * P:(k + 1) * P]
                    low = wT[:, s, v, (KT + k) * P:(KT + k + 1) * P]
                    pe.matmul(bank[:, u.cols], high, xT_tile(u.b, 0, k, u.cols), start=(k == 0), stop=False)
                    pe.matmul(bank[:, u.cols], high, xT_tile(u.b, 1, k, u.cols), start=False, stop=False)
                    mm = pe.matmul(bank[:, u.cols], low, xT_tile(u.b, 0, k, u.cols), start=False, stop=(k == KT - 1))
                mm.then_inc(done, 1)

            def transpose_max(u):
                pe.wait_ge(max_ready, MAX_OPS * u.i + MAX_OPS)
                pe.wait_ge(xlo_ready, KT * u.b + KT)
                for t in u.tiles:
                    tr = pe.transpose(X[:, t * P:(t + 1) * P], m[:, t * P:(t + 1) * P], ident[:, :])
                tr.then_inc(amaxT_psum, 1)

            def spread_scale(u):
                pe.wait_ge(qscale_ready, u.i + 1)
                for t in u.tiles:
                    tr = pe.transpose(S[:, t * P:(t + 1) * P], qscale[:, t:t + 1].to_broadcast([P, P]), ident[:, :])
                tr.then_inc(qscale_psum, 1)

            def down(u, t, bank, steps, first, last):
                for s in steps:
                    mm = pe.matmul(bank[:, :], q[:, s * T + t * P:s * T + (t + 1) * P], dT[:, s, :],
                                   start=(s == first), stop=(s == last))
                if last in steps:
                    mm.then_inc(y_psum, 1)

            def behind(prev, s):
                if s == 0:
                    spread_scale(prev)
                after = down_after(prev)
                if s in after:
                    t = after[s]
                    pe.wait_ge(q_ready, PAIRS * prev.i + PAIRS)
                    if t >= 2:
                        pe.wait_ge(y_done, TT * prev.b + (t - 1))
                    down(prev, t, Y[t % 2], range(FT), 0, FT - 1)

            pe.wait_ge(consts_ready, 1)
            pe.wait_ge(norm_w_loaded, 16)
            for k in range(KT):
                pe.transpose(G[0][:, k * P:(k + 1) * P], nw[:, k, :], ident[:, :])
            pe.wait_ge(cond_loaded, 16)
            pe.transpose(V[0][:, 0:B], cnd, ident[0:B, 0:B]).then_inc(condT_psum, 1)
            pe.wait_ge(condT_ready, 1)
            for k in range(KT):
                mm = pe.matmul(G[1][:, k * B:(k + 1) * B], nwT[:, k, :], cndT, start=True, stop=True)
            mm.then_inc(scl_psum, 1)
            pe.wait_ge(scl_steps, 2)
            pe.transpose(V[1][0:B, 0:P], bmax[:, :], ident[:, :]).then_inc(bmaxT_psum, 1)
            pe.wait_ge(scl_steps, 3)
            pe.transpose(V[0][:, 0:B], brow[:, :].to_broadcast([B, P]), ident[0:B, 0:B]).then_inc(bmax_psum, 1)
            transpose_w(0, 1)
            for k in range(KT):
                transpose_x(0, k, X0[k])
            transpose_w(0, 0)
            for s in range(FT):
                for v in (1, 0):
                    pe.wait_ge(wT_ready, VG * s + 2 - v)
                    up(whole(0), s, v)
                    if s + 1 < FT:
                        transpose_w(s + 1, v)
                    if s in DW_T:
                        transpose_dw(DW_T[s], 1 - v)
                    if s == DW_TOTAL and v:
                        pe.wait_ge(dw_sums, KT)
                        pe.wait_ge(xlo_ready, KT + sum(at < s for at in XPREP_AT_0))
                        pe.matmul(X[:, 0:KT], ones[:, :], dwsum[:, :], start=True, stop=True).then_inc(dw_total_psum, 1)
                if s == DW_TOTAL:
                    pe.wait_ge(dw_scale_ready, 1)
                if s in XPREP_AT_0:
                    transpose_x(1, XPREP_AT_0[s])
            pe.wait_ge(wT_ready, VG * FT)
            pe.wait_ge(dT_ready, 2 * KT)
            with pe.Fori(1, LAST) as b:
                pe.wait_ge(xlo_ready, KT * b + KT)
                for s in range(FT):
                    up(whole(b), s, 1)
                    if s == 0:
                        transpose_max(whole(b - 1))
                    up(whole(b), s, 0)
                    if s in XPREP_AT:
                        transpose_x(b + 1, XPREP_AT[s])
                    behind(whole(b - 1), s)
            pe.wait_ge(xlo_ready, KT * B)
            for prev, u in ((whole(LAST - 1), HALF_A), (HALF_A, HALF_B)):
                for s in range(FT):
                    up(u, s, 1)
                    if s == 0:
                        transpose_max(prev)
                    up(u, s, 0)
                    behind(prev, s)
            transpose_max(HALF_B)
            spread_scale(HALF_B)
            for i in range(PAIRS):
                pe.wait_ge(q_ready, PAIRS * HALF_B.i + i + 1)
                s = 2 * PAIR_ORDER[i]
                for t in HALF_B.tiles:
                    down(HALF_B, t, V[t % 2], (s, s + 1), 2 * PAIR_ORDER[0], 2 * PAIR_ORDER[-1] + 1)


_INS = ["x", "cond_256", "L0_cond_norm_w", "L0_cond_up_w", "L0_cond_down_w"]
_OUTS = [((8, 512, 512), "float32")]


def kernel(**inputs):
    import numpy as _np
    import concourse.bacc as _bacc
    from concourse import mybir as _mybir
    from concourse.bass_utils import run_bass_kernel_spmd as _run

    nc = _bacc.Bacc("TRN2", target_bir_lowering=False, num_devices=1)
    arrays, args = {}, []
    for name in _INS:
        a = _np.ascontiguousarray(inputs[name])
        arrays[f"in_{name}_dram"] = a
        args.append(nc.dram_tensor(f"in_{name}_dram", a.shape, _mybir.dt.from_np(a.dtype), kind="ExternalInput").ap())
    for i, (shape, dtype) in enumerate(_OUTS):
        dt = _mybir.dt.from_np(_np.dtype(dtype))
        args.append(nc.dram_tensor(f"out_{i}_dram", shape, dt, kind="ExternalOutput").ap())
    gated_ffn_program(nc, *args)
    r = _run(nc, [arrays], core_ids=[0])
    return r.results[0]["out_0_dram"]
```
